# Optimizing a Trainium2 kernel written in Bass

```python
import numpy as np
import jax
import jax.numpy as jnp

def _softmax(x, axis=-1):
    return jax.nn.softmax(x, axis=axis)
def _gelu(x):
    return jax.nn.gelu(x, approximate=True)
def _silu(x):
    return jax.nn.silu(x)
def _sigmoid(x):
    return jax.nn.sigmoid(x)
def _layernorm(x, axis=-1, eps=1e-5):
    m = jnp.mean(x, axis=axis, keepdims=True)
    v = jnp.var(x, axis=axis, keepdims=True)
    return (x - m) / jnp.sqrt(v + eps)
def _scatter_add(tgt, idx, src, axis=0):
    return tgt.at[idx].add(src)
def _segment_sum(src, seg, n):
    return jax.ops.segment_sum(src, seg, n)

kernel_name = 'mk_adj_preln_d1_adj_256_28811c'

def setup_inputs(seed: int = 0):
    np.random.seed(seed)
    _w = jnp.asarray
    def _rec_inputs():
        import jax
        import jax.numpy as jnp
        _gk = jax.random.key(seed)
        x = -0.0005207 + 1.001 * jax.random.normal(jax.random.fold_in(_gk, 1), (8192, 256), jnp.float32)
        _w = (1.0 + jnp.arange(8192, dtype=jnp.float32)) ** -0.5
        _w = _w / _w.mean()
        _pij = jnp.clip(0.000488281 * _w[:, None] * _w[None, :], 0.0, 1.0)
        _a = jax.random.uniform(jax.random.fold_in(_gk, 2), (8192, 8192)) < _pij
        adj = _a.astype(jnp.int32)
        return x, adj
    x, adj = _rec_inputs()
    def _L0_gnn_setup():
        import jax, jax.numpy as jnp
        import numpy as np
        N, IN_DIM, OUT_DIM = (8192, 256, 256)
        NEG_INF = -1000000000.0
        key = jax.random.key(seed)
        k1, k2, k3, k4 = jax.random.split(key, 4)
        X = jax.random.normal(k1, (N, IN_DIM), dtype=jnp.float32)
        A = jax.random.randint(k2, (N, N), 0, 2).astype(jnp.int32)
        W_fc = jax.random.normal(k3, (IN_DIM, OUT_DIM), dtype=jnp.float32) * (1.0 / np.sqrt(IN_DIM))
        b_fc = jnp.zeros((OUT_DIM,), dtype=jnp.float32)
        w_att = jax.random.normal(k4, (2 * OUT_DIM,), dtype=jnp.float32) * (1.0 / np.sqrt(2 * OUT_DIM))
        b_att = jnp.zeros((), dtype=jnp.float32)
        return {'X': X, 'A': A, 'W_fc': W_fc, 'b_fc': b_fc, 'w_att': w_att, 'b_att': b_att}
    _L0_gnn_all = _L0_gnn_setup()
    _L0_gnn_in = {k: v for k, v in _L0_gnn_all.items() if k in ('W_fc', 'b_fc', 'w_att', 'b_att', )}
    del _L0_gnn_all

    return {
        "x": x,
        "adj": adj,
        "L0_gnn_W_fc": _L0_gnn_in["W_fc"],
        "L0_gnn_b_fc": _L0_gnn_in["b_fc"],
        "L0_gnn_w_att": _L0_gnn_in["w_att"],
        "L0_gnn_b_att": _L0_gnn_in["b_att"],
    }

def reference(x, adj, L0_gnn_W_fc, L0_gnn_b_fc, L0_gnn_w_att, L0_gnn_b_att):
    import jax
    import jax.numpy as jnp
    def _L0_gnn_ref(X, A, W_fc, b_fc, w_att, b_att):
        import jax, jax.numpy as jnp
        import numpy as np
        N, IN_DIM, OUT_DIM = (8192, 256, 256)
        NEG_INF = -1000000000.0
        H = X @ W_fc + b_fc
        d = H.shape[1]
        s_src = H @ w_att[:d]
        s_dst = H @ w_att[d:]
        scores = s_src[:, None] + s_dst[None, :] + b_att
        scores = jnp.where(A > 0, scores, jnp.float32(NEG_INF))
        alpha = jax.nn.softmax(scores, axis=1)
        return alpha @ H

    h = jnp.maximum(_layernorm(x, axis=-1), 0.0)
    x = x + _L0_gnn_ref(h, adj, L0_gnn_W_fc, L0_gnn_b_fc, L0_gnn_w_att, L0_gnn_b_att)
    return x


_drawn_inputs = setup_inputs


def setup_inputs(seed=0):
    import zlib

    import numpy as np

    out = dict(_drawn_inputs(seed))
    spreads = {'L0_gnn_b_fc': (0.0, 0.1)}
    factors = {}
    for name, (base, spread) in spreads.items():
        noise = np.random.default_rng([zlib.crc32(name.encode()), seed]).standard_normal(out[name].shape)
        drawn = base * np.exp(spread * noise) if base else spread * noise
        out[name] = jnp.asarray(drawn.astype(out[name].dtype))
    for name, factor in factors.items():
        out[name] = (out[name] * factor).astype(out[name].dtype)
    return out
```

```python
from contextlib import ExitStack

import concourse.bass as bass
from concourse import mybir

ALU = mybir.AluOpType
ACT = mybir.ActivationFunctionType
AX = mybir.AxisListType
F32, F16, I32 = mybir.dt.float32, mybir.dt.float16, mybir.dt.int32

P = 128
N = 8192
D = 256
NT = N // P
KH = D // P
LN_EPS = 1e-5
NV = D + 1
NE = D + 2

GT = 4
NG = NT // GT

CW = 2048
CB = CW // P
CPT = N // CW
NC = NT * CPT
PAIR = 2 * CPT
RAW, MSK, ATR = 4, 4, 8
AHEAD = 3
LAG = 2
SPLIT = 4
LO_SCALE = 2048.0
TOP = 32768.0
TINY = 1e-20
RSTD_STEPS = 5
EPI_STEPS = 5


def build(nc, x, adj, w_fc, b_fc, w_att, out):
    with ExitStack() as ctx:
        def sb(name, shape, dt=F32):
            return ctx.enter_context(nc.sbuf_tensor(name, shape, dt))

        def sem(name):
            return ctx.enter_context(nc.semaphore(name))

        h_ext = sb("h_ext", [P, NT, NE])
        raw = sb("raw", [P, RAW, CW], I32)
        mask = sb("mask", [P, MSK, CW], F16)
        at = sb("at", [P, ATR, CW], F16)
        x_in = sb("x_in", [P, 2, GT, D])
        stats = sb("stats", [P, GT, 6])
        mean_var = sb("mean_var", [P, 2, GT, 2])
        std = sb("std", [P, 2, GT])
        rstd = sb("rstd", [P, GT])
        var_eps = sb("var_eps", [P, GT])
        newton = sb("newton", [P, GT])
        y = sb("y", [P, 2, GT, D])
        y_t = sb("y_t", [P, 2, D])
        w_ext = sb("w_ext", [P, KH, NE])
        w_sq = sb("w_sq", [P, KH, D])
        wa_b = sb("wa_b", [P, 2 * D])
        b_ext = sb("b_ext", [P, NE])
        w_prod = sb("w_prod", [P, 2, KH + 1, D])
        ident = sb("ident", [P, P])
        ident16 = sb("ident16", [P, P], F16)
        ones_n = sb("ones_n", [P, P])
        eps = sb("eps", [P, 1])
        h_part = sb("h_part", [P, GT, NE])
        h_sum = sb("h_sum", [P, D])
        h_mean = sb("h_mean", [P, D])
        w_norm_sq = sb("w_norm_sq", [P, 1])
        w_norm = sb("w_norm", [P, 1])
        b_max = sb("b_max", [P, 1])
        h_bound = sb("h_bound", [P, 1])
        inv_bound = sb("inv_bound", [P, 1])
        e_scale = sb("e_scale", [P, 1])
        s_max = sb("s_max", [P, 1])
        m_all = sb("m_all", [P, 1])
        neg_m = sb("neg_m", [P, 1])
        e = sb("e", [P, NT])
        es = sb("es", [P, NT])
        prod = sb("prod", [P, SPLIT, NV])
        rest = sb("rest", [P, SPLIT, NV])
        x_res = sb("x_res", [P, 2, D])
        lo_sum = sb("lo_sum", [P, NV])
        total = sb("total", [P, NV])
        den = sb("den", [P, 1])
        rden = sb("rden", [P, 1])
        lonely = sb("lonely", [P, 1])
        base = sb("base", [P, D])
        y_out = sb("y_out", [P, 2, D])

        tp = ctx.enter_context(nc.psum_tensor("tp", [P, 2, CW], F16))
        acc = ctx.enter_context(nc.psum_tensor("acc", [P, 2, 2, 512], F32))

        parts = h_ext[:].rearrange("p t c -> p (t c)").bitcast(F16).rearrange("p (t h c) -> p t h c", h=2, c=NE)

        weights_in = sem("weights_in")
        x_in_s = [sem(f"x_in_{k}") for k in range(2)]
        raw_in = [sem(f"raw_in_{k}") for k in range(RAW)]
        x_res_in = [sem(f"x_res_in_{k}") for k in range(2)]
        stored = [sem(f"stored_{k}") for k in range(2)]
        ident_ready = sem("ident_ready")
        consts = sem("consts")
        ident16_ready = sem("ident16_ready")
        w_ready = sem("w_ready")
        w_sq_ready = sem("w_sq_ready")
        norms_psum = sem("norms_psum")
        norm_max = sem("norm_max")
        norm_root = sem("norm_root")
        bound_step = sem("bound_step")
        stats_done = sem("stats_done")
        var_ready = sem("var_ready")
        std_ready = sem("std_ready")
        rstd_step = sem("rstd_step")
        y_ready = sem("y_ready")
        yt_psum = sem("yt_psum")
        yt_ready = sem("yt_ready")
        h_psum = sem("h_psum")
        h_ready = sem("h_ready")
        part_sum = sem("part_sum")
        h_sum_ready = sem("h_sum_ready")
        h_mean_psum = sem("h_mean_psum")
        h_mean_ready = sem("h_mean_ready")
        s_max_ready = sem("s_max_ready")
        m_ready = sem("m_ready")
        neg_m_ready = sem("neg_m_ready")
        e_ready = sem("e_ready")
        es_ready = sem("es_ready")
        prod_ready = sem("prod_ready")
        hi_ready = sem("hi_ready")
        rest_ready = sem("rest_ready")
        split_done = sem("split_done")
        masked = sem("masked")
        transposed = sem("transposed")
        evacuated = sem("evacuated")
        summed = sem("summed")
        epi_step = sem("epi_step")
        acc_read = sem("acc_read")
        out_ready = sem("out_ready")

        x_groups = x.rearrange("(g t p) d -> g p t d", t=GT, p=P)
        x_tiles = x.rearrange("(t p) d -> t p d", p=P)
        out_tiles = out.rearrange("(t p) d -> t p d", p=P)
        adj_tiles = adj.rearrange("(t p) c -> t p c", p=P)

        def wait(eng, s, count):
            if not isinstance(count, int) or count > 0:
                eng.wait_ge(s, count)

        block = ctx.enter_context(nc.Block())

        @block.sync
        def _(sp):
            sp.dma_start(w_ext[:, :, 0:D], w_fc.rearrange("(k p) d -> p k d", p=P)).then_inc(weights_in, 16)
            sp.dma_start(wa_b[:], w_att.partition_broadcast(P)).then_inc(weights_in, 16)
            sp.dma_start(b_ext[:, 0:D], b_fc.partition_broadcast(P)).then_inc(weights_in, 16)

            def load_x(w):
                for k in range(2):
                    wait(sp, y_ready, GT * (2 * w + k - 1))
                    sp.dma_start(x_in[:, k], x_groups[2 * w + k]).then_inc(x_in_s[k], 16)

            def load_chunk(u, half, q):
                wait(sp, masked, PAIR * u + CPT * half + q - RAW + 1)
                sp.dma_start(raw[:, q % RAW], adj_tiles[2 * u + half, :, q * CW:(q + 1) * CW]).then_inc(raw_in[q % RAW], 16)

            load_x(0)
            for w in range(1, CPT + 1):
                load_x(w)
                load_chunk(0, 0, w - 1)
            with sp.Fori(CPT + 1, NG // 2) as w:
                load_x(w)

            def store(i, slot):
                wait(sp, out_ready, i + 1)
                sp.dma_start(out_tiles[i], y_out[:, slot]).then_inc(stored[slot], 16)

            def load_residual(i, slot):
                wait(sp, out_ready, i - 1)
                sp.dma_start(x_res[:, slot], x_tiles[i]).then_inc(x_res_in[slot], 16)

            def row_tile(u, half, first=0):
                i = 2 * u + half
                for q in range(first, CPT):
                    load_chunk(u, half, q)
                if not isinstance(i, int) or i >= 3:
                    store(i - 3, 1 - half)
                if not isinstance(i, int) or i >= 1:
                    load_residual(i - 1, 1 - half)

            row_tile(0, 0, first=CPT)
            row_tile(0, 1)
            row_tile(1, 0)
            row_tile(1, 1)
            with sp.Fori(2, NT // 2) as u:
                for half in range(2):
                    row_tile(u, half)
            store(NT - 3, 1)
            load_residual(NT - 1, 1)
            store(NT - 2, 0)
            store(NT - 1, 1)
            for slot in range(2):
                sp.wait_ge(stored[slot], 16 * (NT // 2))

        @block.gpsimd
        def _(pool):
            nc.gpsimd.memset(ident[:], 0.0).then_inc(ident_ready, 1)
            pool.wait_ge(ident_ready, 1)
            nc.gpsimd.affine_select(out=ident[:], in_=ident[:], compare_op=ALU.not_equal, fill=1.0, base=0,
                                    pattern=[[-1, P]], channel_multiplier=1).then_inc(ident_ready, 1)
            pool.wait_ge(h_ready, GT)
            nc.gpsimd.tensor_copy(h_part[:], h_ext[:, 0:GT]).then_inc(part_sum, 1)
            with pool.Fori(1, NG) as g:
                pool.wait_ge(h_ready, GT * (g + 1))
                pool.wait_ge(part_sum, g)
                nc.gpsimd.tensor_tensor(h_part[:], h_part[:], h_ext[:, bass.ds(g * GT, GT)], ALU.add).then_inc(part_sum, 1)
            pool.wait_ge(s_max_ready, 1)
            nc.gpsimd.partition_all_reduce(m_all[:], s_max[:], P, bass.bass_isa.ReduceOp.max).then_inc(m_ready, 1)

        @block.tensor
        def _(pe):
            pe.wait_ge(w_sq_ready, 1)
            pe.wait_ge(consts, 2)
            for k in range(KH):
                mm = nc.tensor.matmul(acc[:, 1, 0, 0:D], ones_n[:], w_sq[:, k], start=(k == 0), stop=(k == KH - 1))
            mm.then_inc(norms_psum, 1)
            pe.wait_ge(norm_max, 1)
            pe.wait_ge(ident_ready, 2)
            pe.wait_ge(w_ready, 1)

            def turn(w, m):
                t = 2 * GT * w + m
                slot = (m // GT) % 2
                pe.wait_ge(y_ready, t + 1)
                wait(pe, yt_ready, t - 1)
                for k in range(KH):
                    mm = nc.tensor.transpose(acc[:, 0, m % 2, k * P:(k + 1) * P], y[:, slot, m % GT, k * P:(k + 1) * P], ident[:])
                mm.then_inc(yt_psum, 1)

            def times_w(g, n):
                t = GT * g + n
                pe.wait_ge(yt_ready, t + 1)
                wait(pe, h_ready, t - 1)
                for k in range(KH):
                    mm = nc.tensor.matmul(acc[:, 1, n % 2, 0:NE], y_t[:, n % 2, k * P:(k + 1) * P], w_ext[:, k],
                                          start=(k == 0), stop=(k == KH - 1))
                mm.then_inc(h_psum, 1)

            def two_groups(w, last=False):
                for m in range(2 * GT):
                    g, n = 2 * w + m // GT, m % GT
                    if not (last and m == 2 * GT - 1):
                        turn(w, m + 1)
                    times_w(g, n)

            turn(0, 0)
            two_groups(0)
            with pe.Fori(1, NG // 2 - 1) as w:
                two_groups(w)
            two_groups(NG // 2 - 1, last=True)

            def transpose_chunk(u, c):
                g = PAIR * u + c
                pe.wait_ge(masked, g + 1)
                wait(pe, evacuated, g - 1)
                for b in range(CB):
                    mm = nc.tensor.transpose(tp[:, c % 2, b * P:(b + 1) * P], mask[:, c % MSK, b * P:(b + 1) * P], ident16[:])
                mm.then_inc(transposed, 1)

            def multiply_chunk(u, c):
                g, q, half = PAIR * u + c, c % CPT, c // CPT
                pe.wait_ge(evacuated, g + 1)
                if isinstance(u, int) and u == 0 and half == 0:
                    pe.wait_ge(split_done, CB * (q + 1))
                if q == 0:
                    wait(pe, acc_read, 2 * u + half - 1)
                for b in range(CB):
                    t = q * CB + b
                    for part in range(2):
                        mm = nc.tensor.matmul(acc[:, half, part, 0:NV], at[:, c % ATR, b * P:(b + 1) * P], parts[:, t, part, 0:NV],
                                              start=(t == 0), stop=(t == NT - 1))
                mm.then_inc(summed, 1)

            pe.wait_ge(ident16_ready, 1)
            for c in range(AHEAD):
                transpose_chunk(0, c)
            pe.wait_ge(h_sum_ready, 1)
            nc.tensor.matmul(acc[:, 0, 0, 0:D], ones_n[:], h_sum[:], start=True, stop=True).then_inc(h_mean_psum, 1)
            pe.wait_ge(h_mean_ready, 1)

            def pair(u, last=False):
                for c in range(PAIR):
                    if not (last and c + AHEAD >= PAIR):
                        transpose_chunk(u, c + AHEAD)
                    multiply_chunk(u, c)

            pair(0)
            with pe.Fori(1, NT // 2 - 1) as u:
                pair(u)
            pair(NT // 2 - 1, last=True)

        @block.scalar
        def _(act):
            act.wait_ge(norm_max, 1)
            nc.scalar.activation(w_norm[:], w_norm_sq[:], ACT.Sqrt, scale=float(D * N)).then_inc(norm_root, 1)
            act.wait_ge(consts, 2)

            def group(w, k):
                g = 2 * w + k
                act.wait_ge(var_ready, GT * (g + 1))
                wait(act, rstd_step, RSTD_STEPS * (g - 1))
                nc.scalar.activation(std[:, k], mean_var[:, k, :, 1], ACT.Sqrt, bias=eps[:, 0:1]).then_inc(std_ready, 1)
                for n in range(GT):
                    t = GT * g + n
                    act.wait_ge(yt_psum, t + 1)
                    wait(act, h_psum, t - 1)
                    nc.scalar.activation(y_t[:, n % 2], acc[:, 0, n % 2, 0:D], ACT.Copy).then_inc(yt_ready, 1)

            for k in range(2):
                group(0, k)
            with act.Fori(1, NG // 2) as w:
                for k in range(2):
                    group(w, k)

            def evacuate(u, c):
                g = PAIR * u + c
                act.wait_ge(transposed, g + 1)
                wait(act, summed, g - ATR + 1)
                nc.scalar.activation(at[:, c % ATR], tp[:, c % 2], ACT.Copy).then_inc(evacuated, 1)

            act.wait_ge(neg_m_ready, 1)
            nc.scalar.activation(e[:], h_ext[:, :, D], ACT.Exp, bias=neg_m[:, 0:1]).then_inc(e_ready, 1)
            for c in range(AHEAD):
                evacuate(0, c)

            def product(w, n):
                t = SPLIT * w + n
                wait(act, rest_ready, t - SPLIT + 1)
                nc.scalar.activation(prod[:, n], h_ext[:, t, 0:NV], ACT.Copy, scale=es[:, bass.ds(t, 1)]).then_inc(prod_ready, 1)

            def low_part(w, n):
                t = SPLIT * w + n
                act.wait_ge(rest_ready, t + 1)
                nc.scalar.activation(parts[:, t, 1, 0:NV], rest[:, n], ACT.Copy, scale=LO_SCALE).then_inc(split_done, 1)

            act.wait_ge(es_ready, 2)
            for n in range(SPLIT):
                product(0, n)
            for q in range(CPT):
                last = q == CPT - 1
                with act.Fori(q * CB // SPLIT, (q + 1) * CB // SPLIT - last) as w:
                    for n in range(SPLIT):
                        low_part(w, n)
                        product(w + 1, n)
                if last:
                    for n in range(SPLIT):
                        low_part(NT // SPLIT - 1, n)
                evacuate(0, AHEAD + q)

            for c in range(AHEAD + CPT, PAIR):
                evacuate(0, c)
            with act.Fori(1, NT // 2) as u:
                for c in range(PAIR):
                    evacuate(u, c)

        @block.vector
        def _(dve):
            nc.vector.memset(ones_n[:], 1.0 / N).then_inc(consts, 1)
            nc.vector.memset(eps[:], LN_EPS).then_inc(consts, 1)
            dve.wait_ge(weights_in, 48)
            nc.vector.tensor_tensor(w_sq[:], w_ext[:, :, 0:D], w_ext[:, :, 0:D], ALU.mult).then_inc(w_sq_ready, 1)
            for j, half in ((0, 1), (1, 0)):
                for r, row in enumerate((w_ext[:, 0], w_ext[:, 1], b_ext[:])):
                    last = nc.vector.tensor_tensor_reduce(out=w_prod[:, j, r], in0=row[:, 0:D], in1=wa_b[:, half * D:(half + 1) * D],
                                                          scale=1.0, scalar=0.0, op0=ALU.mult, op1=ALU.add,
                                                          accum_out=row[:, D + j:D + j + 1])
            last.then_inc(w_ready, 1)
            dve.wait_ge(norms_psum, 1)
            nc.vector.tensor_reduce(w_norm_sq[:], acc[:, 1, 0, 0:D], AX.X, ALU.max).then_inc(norm_max, 1)
            nc.vector.tensor_reduce(b_max[:], b_ext[:, 0:D], AX.X, ALU.max, apply_absolute_value=True).then_inc(bound_step, 1)
            dve.wait_ge(norm_root, 1)
            dve.wait_ge(bound_step, 1)
            nc.vector.tensor_scalar(h_bound[:], w_norm[:], b_max[:, 0:1], TINY, ALU.add, ALU.max).then_inc(bound_step, 1)
            dve.wait_ge(bound_step, 2)
            nc.vector.reciprocal(inv_bound[:], h_bound[:]).then_inc(bound_step, 1)
            dve.wait_ge(bound_step, 3)
            nc.vector.tensor_scalar(e_scale[:], inv_bound[:], TOP, None, ALU.mult).then_inc(bound_step, 1)
            dve.wait_ge(ident_ready, 2)
            nc.vector.tensor_copy(ident16[:], ident[:]).then_inc(ident16_ready, 1)

            def invert_std(g, k):
                wait(dve, h_ready, GT * g)
                dve.wait_ge(std_ready, g + 1)
                nc.vector.reciprocal(rstd[:], std[:, k]).then_inc(rstd_step, 1)

            def normalise(w, k):
                g = 2 * w + k
                dve.wait_ge(x_in_s[k], 16 * (w + 1))
                for n in range(GT):
                    nc.vector.bn_stats(stats[:, n], x_in[:, k, n]).then_inc(stats_done, 1)
                dve.wait_ge(stats_done, GT * (g + 1))
                if not isinstance(g, int) or g > 0:
                    invert_std(g - 1, 1 - k)
                for n in range(GT):
                    nc.vector.bn_aggr(mean_var[:, k, n], stats[:, n]).then_inc(var_ready, 1)
                dve.wait_ge(var_ready, GT * (g + 1))
                wait(dve, yt_psum, GT * (g - 1))
                for n in range(GT):
                    nc.vector.tensor_scalar(y[:, k, n], x_in[:, k, n], mean_var[:, k, n, 0:1], 0.0,
                                            ALU.subtract, ALU.max).then_inc(y_ready, 1)

            def finish(w, k):
                g = 2 * w + k
                dve.wait_ge(rstd_step, RSTD_STEPS * g + 1)
                nc.vector.tensor_scalar(var_eps[:], mean_var[:, k, :, 1], LN_EPS, None, ALU.add).then_inc(rstd_step, 1)
                nc.vector.tensor_tensor(newton[:], rstd[:], rstd[:], ALU.mult).then_inc(rstd_step, 1)
                dve.wait_ge(rstd_step, RSTD_STEPS * g + 3)
                nc.vector.scalar_tensor_tensor(newton[:], newton[:], -0.5, var_eps[:], ALU.mult, ALU.mult).then_inc(rstd_step, 1)
                dve.wait_ge(rstd_step, RSTD_STEPS * g + 4)
                nc.vector.scalar_tensor_tensor(rstd[:], newton[:], 1.5, rstd[:], ALU.add, ALU.mult).then_inc(rstd_step, 1)
                dve.wait_ge(rstd_step, RSTD_STEPS * g + 5)
                for n in range(GT):
                    t = GT * g + n
                    dve.wait_ge(h_psum, t + 1)
                    nc.vector.scalar_tensor_tensor(h_ext[:, t], acc[:, 1, n % 2, 0:NE], rstd[:, n:n + 1], b_ext[:],
                                                   ALU.mult, ALU.add).then_inc(h_ready, 1)

            normalise(0, 0)
            normalise(0, 1)
            finish(0, 0)
            with dve.Fori(1, NG // 2) as w:
                normalise(w, 0)
                finish(w - 1, 1)
                normalise(w, 1)
                finish(w, 0)
            invert_std(NG - 1, 1)
            finish(NG // 2 - 1, 1)

            dve.wait_ge(h_ready, NT)
            nc.vector.tensor_reduce(s_max[:], h_ext[:, :, D], AX.X, ALU.max).then_inc(s_max_ready, 1)

            def make_mask(u, c):
                g = PAIR * u + c
                dve.wait_ge(raw_in[c % RAW], 16 * (PAIR // RAW * u + c // RAW + 1))
                wait(dve, transposed, g - MSK + 1)
                nc.vector.tensor_scalar(mask[:, c % MSK], raw[:, c % RAW], 0.0, None, ALU.is_gt).then_inc(masked, 1)

            make_mask(0, 0)
            dve.wait_ge(part_sum, NG)
            nc.vector.tensor_reduce(h_sum[:], h_part[:, :, 0:D].rearrange("p t d -> p d t"), AX.X, ALU.add).then_inc(h_sum_ready, 1)
            dve.wait_ge(m_ready, 1)
            nc.vector.tensor_scalar(neg_m[:], m_all[:], -1.0, None, ALU.mult).then_inc(neg_m_ready, 1)
            make_mask(0, 1)
            dve.wait_ge(e_ready, 1)
            dve.wait_ge(bound_step, 4)
            nc.vector.tensor_scalar(es[:], e[:], e_scale[:, 0:1], None, ALU.mult).then_inc(es_ready, 1)
            nc.vector.tensor_scalar(h_ext[:, :, D], e[:], 0.0, h_bound[:, 0:1], ALU.mult, ALU.add).then_inc(es_ready, 1)
            make_mask(0, 2)
            make_mask(0, 3)
            dve.wait_ge(h_mean_psum, 1)
            nc.vector.tensor_copy(h_mean[:], acc[:, 0, 0, 0:D]).then_inc(h_mean_ready, 1)

            def high_part(w, n):
                t = SPLIT * w + n
                dve.wait_ge(prod_ready, t + 1)
                nc.vector.tensor_copy(parts[:, t, 0, 0:NV], prod[:, n % SPLIT]).then_inc(hi_ready, 1)

            def leave_rest(w, n):
                t = SPLIT * w + n
                dve.wait_ge(hi_ready, t + 1)
                wait(dve, split_done, t - SPLIT + 1)
                nc.vector.tensor_tensor(rest[:, n], prod[:, n], parts[:, t, 0, 0:NV], ALU.subtract).then_inc(rest_ready, 1)

            def split_four(w, last=False):
                for n in range(SPLIT):
                    if not (last and n == SPLIT - 1):
                        high_part(w, n + 1)
                    leave_rest(w, n)

            high_part(0, 0)
            split_four(0)
            for q in range(CPT):
                last = q == CPT - 1
                with dve.Fori(max(1, q * CB // SPLIT), (q + 1) * CB // SPLIT - last) as w:
                    split_four(w)
                if last:
                    split_four(NT // SPLIT - 1, last=True)
                make_mask(0, CPT + q)

            def epilogue(u, half):
                i = 2 * u + half
                dve.wait_ge(summed, CPT * (i + 1))
                nc.vector.tensor_scalar(lo_sum[:], acc[:, half, 1, 0:NV], 1.0 / LO_SCALE, None, ALU.mult).then_inc(epi_step, 1)
                dve.wait_ge(epi_step, EPI_STEPS * i + 1)
                nc.vector.tensor_tensor(total[:], acc[:, half, 0, 0:NV], lo_sum[:], ALU.add).then_inc(acc_read, 1)
                dve.wait_ge(acc_read, i + 1)
                nc.vector.tensor_scalar(den[:], total[:, D:NV], TINY, inv_bound[:, 0:1], ALU.max, ALU.mult).then_inc(epi_step, 1)
                nc.vector.tensor_scalar(lonely[:], total[:, D:NV], 0.0, None, ALU.is_equal).then_inc(epi_step, 1)
                dve.wait_ge(epi_step, EPI_STEPS * i + 3)
                nc.vector.reciprocal(rden[:], den[:]).then_inc(epi_step, 1)
                dve.wait_ge(x_res_in[half], 16 * (u + 1))
                nc.vector.scalar_tensor_tensor(base[:], h_mean[:], lonely[:, 0:1], x_res[:, half], ALU.mult, ALU.add).then_inc(epi_step, 1)
                dve.wait_ge(epi_step, EPI_STEPS * i + 5)
                wait(dve, stored[half], 16 * u)
                nc.vector.scalar_tensor_tensor(y_out[:, half], total[:, 0:D], rden[:, 0:1], base[:], ALU.mult, ALU.add).then_inc(out_ready, 1)

            def pair(u):
                for half in range(2):
                    for q in range(CPT):
                        make_mask(u, CPT * half + q)
                        if q == 0:
                            epilogue(u - LAG // 2, half)

            pair(1)
            with dve.Fori(2, NT // 2) as u:
                pair(u)
            epilogue(NT // 2 - 1, 0)
            epilogue(NT // 2 - 1, 1)


_INS = ["x", "adj", "L0_gnn_W_fc", "L0_gnn_b_fc", "L0_gnn_w_att"]


def kernel(**inputs):
    import numpy as np
    import concourse.bacc as bacc
    from concourse.bass_utils import run_bass_kernel_spmd

    nc = bacc.Bacc("TRN2", target_bir_lowering=False, num_devices=1)
    arrays, args = {}, []
    for name in _INS:
        a = np.ascontiguousarray(inputs[name])
        arrays[name] = a
        args.append(nc.dram_tensor(name, a.shape, mybir.dt.from_np(a.dtype), kind="ExternalInput").ap())
    args.append(nc.dram_tensor("out", (N, D), F32, kind="ExternalOutput").ap())
    build(nc, *args)
    r = run_bass_kernel_spmd(nc, [arrays], core_ids=[0])
    return r.results[0]["out"]
```

```python
from contextlib import ExitStack

import concourse.bass as bass
from concourse import mybir

ALU = mybir.AluOpType
ACT = mybir.ActivationFunctionType
AX = mybir.AxisListType
F32, F16, I32 = mybir.dt.float32, mybir.dt.float16, mybir.dt.int32

P = 128
N = 8192
D = 256
NT = N // P
KH = D // P
LN_EPS = 1e-5
NV = D + 1
NE = D + 2

GT = 4
NG = NT // GT

Q = 4
QP = P // Q
F = P // QP
CW = N // Q
CWORDS = CW // 2
PAIRS = NT // 2
HALVES = 2
RAW = 2 * F
SHIFT = 4
RESTS = 4
LO_SCALE = 2048.0
TOP = 32768.0
TINY = 1e-20
RSTD_STEPS = 5
EPI_STEPS = 5


def build(nc, x, adj, w_fc, b_fc, w_att, out):
    with ExitStack() as ctx:
        def sb(name, shape, dt=F32):
            return ctx.enter_context(nc.sbuf_tensor(name, shape, dt))

        def sem(name):
            return ctx.enter_context(nc.semaphore(name))

        h_mem = sb("h_mem", [P, SHIFT + NT, NE])
        raw = sb("raw", [P, RAW, CW], I32)
        mask = sb("mask", [P, F, CW], F16)
        turned = sb("turned", [P, 2, CWORDS // QP, F, QP], I32)
        stats = sb("stats", [P, GT, 6])
        mean_var = sb("mean_var", [P, 2, GT, 2])
        std = sb("std", [P, 2, GT])
        rstd = sb("rstd", [P, GT])
        var_eps = sb("var_eps", [P, GT])
        newton = sb("newton", [P, GT])
        y_t = sb("y_t", [P, 2, D])
        w_ext = sb("w_ext", [P, KH, NE])
        wa_b = sb("wa_b", [P, 2 * D])
        b_ext = sb("b_ext", [P, NE])
        ident = sb("ident", [P, P])
        ident16 = sb("ident16", [P, P], F16)
        ones_n = sb("ones_n", [P, P])
        eps = sb("eps", [P, 1])
        h_sum = sb("h_sum", [P, D])
        h_mean = sb("h_mean", [P, D])
        w_norm_sq = sb("w_norm_sq", [P, 1])
        w_norm = sb("w_norm", [P, 1])
        b_max = sb("b_max", [P, 1])
        h_bound = sb("h_bound", [P, 1])
        inv_bound = sb("inv_bound", [P, 1])
        e_scale = sb("e_scale", [P, 1])
        s_max = sb("s_max", [P, 1])
        m_all = sb("m_all", [P, 1])
        neg_m = sb("neg_m", [P, 1])
        e = sb("e", [P, NT])
        es = sb("es", [P, NT])
        rest = sb("rest", [P, RESTS, NV])
        x_res = sb("x_res", [P, 2, D])
        lo_sum = sb("lo_sum", [P, NV])
        total = sb("total", [P, NV])
        den = sb("den", [P, 1])
        rden = sb("rden", [P, 1])
        lonely = sb("lonely", [P, 1])
        base = sb("base", [P, D])
        y_out = sb("y_out", [P, 2, D])

        h_ext = h_mem[:, SHIFT:]
        parts = h_mem[:].rearrange("p t c -> p (t c)").bitcast(F16).rearrange("p (t h c) -> p t h c", h=2, c=NE)
        words = mask[:].rearrange("p f c -> p (f c)").bitcast(I32).rearrange("p (f a t) -> p f t a", f=F, a=QP)
        at = turned[:].rearrange("p h t f b -> p (h t f b)").bitcast(F16).rearrange("p (h t m r) -> p h t m r", h=2, m=P, r=2)
        y = raw[:, RAW - 2].bitcast(F32).rearrange("p (k n d) -> p k n d", k=2, n=GT)
        x_in = raw[:, RAW - 1].bitcast(F32).rearrange("p (k n d) -> p k n d", k=2, n=GT)
        spare = turned[:, 1].rearrange("p t f b -> p (t f b)").bitcast(F32)
        h_part = spare[:, 0:GT * NE].rearrange("p (n c) -> p n c", n=GT)
        w_sq = spare[:, 1100:1100 + KH * D].rearrange("p (k d) -> p k d", k=KH)
        w_prod = spare[:, 2000:2000 + 6 * D].rearrange("p (j r d) -> p j r d", j=2, r=3)

        acc = ctx.enter_context(nc.psum_tensor("acc", [P, 2, 2, 512], F32))
        h_acc = ctx.enter_context(nc.psum_tensor("h_acc", [P, GT, 512], F32))

        weights_in = sem("weights_in")
        x_in_s = [sem(f"x_in_{k}") for k in range(2)]
        raw_in = [sem(f"raw_in_{k}") for k in range(RAW // 2)]
        x_res_in = [sem(f"x_res_in_{k}") for k in range(2)]
        stored = [sem(f"stored_{k}") for k in range(2)]
        ident_ready = sem("ident_ready")
        consts = sem("consts")
        ident16_ready = sem("ident16_ready")
        w_ready = sem("w_ready")
        w_sq_ready = sem("w_sq_ready")
        norms_psum = sem("norms_psum")
        norm_max = sem("norm_max")
        norm_root = sem("norm_root")
        bound_step = sem("bound_step")
        stats_done = sem("stats_done")
        var_ready = sem("var_ready")
        std_ready = sem("std_ready")
        rstd_step = sem("rstd_step")
        y_ready = sem("y_ready")
        yt_psum = sem("yt_psum")
        yt_ready = sem("yt_ready")
        h_psum = sem("h_psum")
        h_ready = sem("h_ready")
        part_sum = sem("part_sum")
        h_sum_ready = sem("h_sum_ready")
        h_mean_psum = sem("h_mean_psum")
        h_mean_ready = sem("h_mean_ready")
        s_max_ready = sem("s_max_ready")
        m_ready = sem("m_ready")
        neg_m_ready = sem("neg_m_ready")
        e_ready = sem("e_ready")
        es_ready = sem("es_ready")
        hi_ready = sem("hi_ready")
        rest_ready = sem("rest_ready")
        split_done = sem("split_done")
        masked = sem("masked")
        transposed = sem("transposed")
        summed = sem("summed")
        epi_step = sem("epi_step")
        acc_read = sem("acc_read")
        out_ready = sem("out_ready")

        x_groups = x.rearrange("(p g n) d -> g p n d", p=P, n=GT)
        x_tiles = x.rearrange("(i p) d -> i p d", p=P)
        out_tiles = out.rearrange("(i p) d -> i p d", p=P)
        adj_quarters = adj.rearrange("(i f b) (q c) -> i q b f c", f=F, b=QP, q=Q)

        def load_adjacency(eng, i, slot, half, quadrants):
            for q in quadrants:
                eng.dma_start(raw[q * QP:(q + 1) * QP, slot:slot + 2],
                              adj_quarters[i, q, :, 2 * half:2 * half + 2]).then_inc(raw_in[slot // 2], 16)

        def wait(eng, s, count):
            if not isinstance(count, int) or count > 0:
                eng.wait_ge(s, count)

        block = ctx.enter_context(nc.Block())

        @block.sync
        def _(sp):
            sp.dma_start(w_ext[:, :, 0:D], w_fc.rearrange("(k p) d -> p k d", p=P)).then_inc(weights_in, 16)
            sp.dma_start(wa_b[:], w_att.partition_broadcast(P)).then_inc(weights_in, 16)
            sp.dma_start(b_ext[:, 0:D], b_fc.partition_broadcast(P)).then_inc(weights_in, 16)

            def load_x(w):
                for k in range(2):
                    wait(sp, y_ready, GT * (2 * w + k - 1))
                    sp.dma_start(x_in[:, k], x_groups[2 * w + k]).then_inc(x_in_s[k], 16)

            def load_tile(u, parity):
                for half in range(HALVES):
                    wait(sp, masked, F * (2 * u + parity - 2) + 2 * half + 2)
                    load_adjacency(sp, 2 * u + parity, F * parity + 2 * half, half, (0, 2))

            load_x(0)
            load_x(1)
            load_adjacency(sp, 0, 0, 0, (0, 2))
            load_x(2)
            load_adjacency(sp, 0, 2, 1, (0, 2))
            load_x(3)
            load_adjacency(sp, 1, 4, 0, (0, 2))
            with sp.Fori(4, NG // 2) as w:
                load_x(w)
            sp.wait_ge(yt_psum, NT)
            load_adjacency(sp, 1, 6, 1, (0, 2))

            def store(i, slot):
                sp.wait_ge(out_ready, i + 1)
                sp.dma_start(out_tiles[i], y_out[:, slot]).then_inc(stored[slot], 16)

            def load_residual(i, slot):
                wait(sp, out_ready, i - 1)
                sp.dma_start(x_res[:, slot], x_tiles[i]).then_inc(x_res_in[slot], 16)

            for parity in range(2):
                load_tile(1, parity)
                load_residual(parity, parity)
            with sp.Fori(2, PAIRS) as u:
                for parity in range(2):
                    load_tile(u, parity)
                    store(2 * u + parity - 4, parity)
                    load_residual(2 * u + parity - 2, parity)
            for i in range(NT - 4, NT):
                store(i, i % 2)
                if i + 2 < NT:
                    load_residual(i + 2, i % 2)
            for slot in range(2):
                sp.wait_ge(stored[slot], 16 * (NT // 2))

        @block.gpsimd
        def _(pool):
            nc.gpsimd.memset(ident[:], 0.0).then_inc(ident_ready, 1)
            pool.wait_ge(ident_ready, 1)
            nc.gpsimd.affine_select(out=ident[:], in_=ident[:], compare_op=ALU.not_equal, fill=1.0, base=0,
                                    pattern=[[-1, P]], channel_multiplier=1).then_inc(ident_ready, 1)
            pool.wait_ge(h_ready, GT)
            nc.gpsimd.tensor_copy(h_part[:], h_ext[:, 0:GT]).then_inc(part_sum, 1)
            with pool.Fori(1, NG) as g:
                pool.wait_ge(h_ready, GT * (g + 1))
                pool.wait_ge(part_sum, g)
                nc.gpsimd.tensor_tensor(h_part[:], h_part[:], h_ext[:, bass.ds(g * GT, GT)], ALU.add).then_inc(part_sum, 1)
            pool.wait_ge(s_max_ready, 1)
            nc.gpsimd.partition_all_reduce(m_all[:], s_max[:], P, bass.bass_isa.ReduceOp.max).then_inc(m_ready, 1)

        @block.tensor
        def _(pe):
            pe.wait_ge(w_sq_ready, 1)
            pe.wait_ge(consts, 2)
            for k in range(KH):
                mm = nc.tensor.matmul(acc[:, 1, 0, 0:D], ones_n[:], w_sq[:, k], start=(k == 0), stop=(k == KH - 1))
            mm.then_inc(norms_psum, 1)
            pe.wait_ge(norm_max, 1)
            pe.wait_ge(ident_ready, 2)
            pe.wait_ge(w_ready, 1)

            def turn(w, m):
                t = 2 * GT * w + m
                pe.wait_ge(y_ready, t + 1)
                wait(pe, yt_ready, t - 1)
                for k in range(KH):
                    mm = nc.tensor.transpose(acc[:, 0, m % 2, k * P:(k + 1) * P],
                                             y[:, m // GT % 2, m % GT, k * P:(k + 1) * P], ident[:])
                mm.then_inc(yt_psum, 1)

            def times_w(w, m):
                t = 2 * GT * w + m
                pe.wait_ge(yt_ready, t + 1)
                wait(pe, h_ready, t - GT + 1)
                for k in range(KH):
                    mm = nc.tensor.matmul(h_acc[:, m % GT, 0:NE], y_t[:, m % 2, k * P:(k + 1) * P], w_ext[:, k],
                                          start=(k == 0), stop=(k == KH - 1))
                mm.then_inc(h_psum, 1)

            def two_groups(w, last=False):
                for m in range(2 * GT):
                    if not (last and m == 2 * GT - 1):
                        turn(w, m + 1)
                    times_w(w, m)

            turn(0, 0)
            two_groups(0)
            with pe.Fori(1, NG // 2 - 1) as w:
                two_groups(w)
            two_groups(NG // 2 - 1, last=True)

            pe.wait_ge(h_sum_ready, 1)
            nc.tensor.matmul(acc[:, 1, 0, 0:D], ones_n[:], h_sum[:], start=True, stop=True).then_inc(h_mean_psum, 1)
            pe.wait_ge(h_mean_ready, 1)

            def product(parity, t, part):
                return nc.tensor.matmul(acc[:, parity, part, 0:NV], at[:, parity, t // 2, :, t % 2], parts[:, t, part, 0:NV],
                                        start=(t == 0), stop=(t == NT - 1))

            pe.wait_ge(transposed, 2 * F)
            for t in range(NT):
                if t % 4 == 0:
                    pe.wait_ge(split_done, t + 4)
                for parity in range(2):
                    for part in range(2):
                        mm = product(parity, t, part)
                    if t == NT - 1:
                        mm.then_inc(summed, 1)

            with pe.Fori(1, PAIRS) as u:
                for parity in range(2):
                    i = 2 * u + parity
                    pe.wait_ge(transposed, F * (i + 1))
                    pe.wait_ge(acc_read, i - 1)
                    for t in range(NT):
                        for part in range(2):
                            mm = product(parity, t, part)
                    mm.then_inc(summed, 1)

        @block.scalar
        def _(act):
            act.wait_ge(norm_max, 1)
            nc.scalar.activation(w_norm[:], w_norm_sq[:], ACT.Sqrt, scale=float(D * N)).then_inc(norm_root, 1)
            act.wait_ge(consts, 2)

            def group(w, k):
                g = 2 * w + k
                act.wait_ge(var_ready, GT * (g + 1))
                wait(act, rstd_step, RSTD_STEPS * (g - 1))
                nc.scalar.activation(std[:, k], mean_var[:, k, :, 1], ACT.Sqrt, bias=eps[:, 0:1]).then_inc(std_ready, 1)
                for n in range(GT):
                    t = GT * g + n
                    act.wait_ge(yt_psum, t + 1)
                    wait(act, h_psum, t - 1)
                    nc.scalar.activation(y_t[:, n % 2], acc[:, 0, n % 2, 0:D], ACT.Copy).then_inc(yt_ready, 1)

            for k in range(2):
                group(0, k)
            for i, half in ((0, 0), (0, 1), (1, 0)):
                load_adjacency(act, i, F * i + 2 * half, half, (1, 3))
            with act.Fori(1, NG // 2) as w:
                for k in range(2):
                    group(w, k)
            act.wait_ge(yt_psum, NT)
            load_adjacency(act, 1, 6, 1, (1, 3))

            act.wait_ge(neg_m_ready, 1)
            nc.scalar.activation(e[:], h_ext[:, :, D], ACT.Exp, bias=neg_m[:, 0:1]).then_inc(e_ready, 1)

            def high_part(t):
                wait(act, rest_ready, t - SHIFT + 1)
                nc.scalar.activation(parts[:, t, 0, 0:NV], h_ext[:, t, 0:NV], ACT.Copy, scale=es[:, bass.ds(t, 1)]).then_inc(hi_ready, 1)

            act.wait_ge(es_ready, 2)
            for n in range(SHIFT):
                high_part(n)
            with act.Fori(1, NT // SHIFT) as w:
                for n in range(SHIFT):
                    high_part(SHIFT * w + n)

            with act.Fori(1, PAIRS) as u:
                for parity in range(2):
                    for half in range(HALVES):
                        act.wait_ge(masked, F * (2 * u + parity - 2) + 2 * half + 2)
                        load_adjacency(act, 2 * u + parity, F * parity + 2 * half, half, (1, 3))

        @block.vector
        def _(dve):
            nc.vector.memset(ones_n[:], 1.0 / N).then_inc(consts, 1)
            nc.vector.memset(eps[:], LN_EPS).then_inc(consts, 1)
            dve.wait_ge(weights_in, 48)
            nc.vector.tensor_tensor(w_sq[:], w_ext[:, :, 0:D], w_ext[:, :, 0:D], ALU.mult).then_inc(w_sq_ready, 1)
            for j, half in ((0, 1), (1, 0)):
                for r, row in enumerate((w_ext[:, 0], w_ext[:, 1], b_ext[:])):
                    last = nc.vector.tensor_tensor_reduce(out=w_prod[:, j, r], in0=row[:, 0:D], in1=wa_b[:, half * D:(half + 1) * D],
                                                          scale=1.0, scalar=0.0, op0=ALU.mult, op1=ALU.add,
                                                          accum_out=row[:, D + j:D + j + 1])
            last.then_inc(w_ready, 1)
            dve.wait_ge(norms_psum, 1)
            nc.vector.tensor_reduce(w_norm_sq[:], acc[:, 1, 0, 0:D], AX.X, ALU.max).then_inc(norm_max, 1)
            nc.vector.tensor_reduce(b_max[:], b_ext[:, 0:D], AX.X, ALU.max, apply_absolute_value=True).then_inc(bound_step, 1)
            dve.wait_ge(norm_root, 1)
            dve.wait_ge(bound_step, 1)
            nc.vector.tensor_scalar(h_bound[:], w_norm[:], b_max[:, 0:1], TINY, ALU.add, ALU.max).then_inc(bound_step, 1)
            dve.wait_ge(bound_step, 2)
            nc.vector.reciprocal(inv_bound[:], h_bound[:]).then_inc(bound_step, 1)
            dve.wait_ge(bound_step, 3)
            nc.vector.tensor_scalar(e_scale[:], inv_bound[:], TOP, None, ALU.mult).then_inc(bound_step, 1)
            dve.wait_ge(ident_ready, 2)
            nc.vector.tensor_copy(ident16[:], ident[:]).then_inc(ident16_ready, 1)

            def invert_std(g, k):
                wait(dve, h_ready, GT * g)
                dve.wait_ge(std_ready, g + 1)
                nc.vector.reciprocal(rstd[:], std[:, k]).then_inc(rstd_step, 1)

            def normalise(w, k):
                g = 2 * w + k
                dve.wait_ge(x_in_s[k], 16 * (w + 1))
                for n in range(GT):
                    nc.vector.bn_stats(stats[:, n], x_in[:, k, n]).then_inc(stats_done, 1)
                dve.wait_ge(stats_done, GT * (g + 1))
                if not isinstance(g, int) or g > 0:
                    invert_std(g - 1, 1 - k)
                for n in range(GT):
                    nc.vector.bn_aggr(mean_var[:, k, n], stats[:, n]).then_inc(var_ready, 1)
                dve.wait_ge(var_ready, GT * (g + 1))
                wait(dve, yt_psum, GT * (g - 1))
                for n in range(GT):
                    nc.vector.tensor_scalar(y[:, k, n], x_in[:, k, n], mean_var[:, k, n, 0:1], 0.0,
                                            ALU.subtract, ALU.max).then_inc(y_ready, 1)

            def finish(w, k):
                g = 2 * w + k
                dve.wait_ge(rstd_step, RSTD_STEPS * g + 1)
                nc.vector.tensor_scalar(var_eps[:], mean_var[:, k, :, 1], LN_EPS, None, ALU.add).then_inc(rstd_step, 1)
                nc.vector.tensor_tensor(newton[:], rstd[:], rstd[:], ALU.mult).then_inc(rstd_step, 1)
                dve.wait_ge(rstd_step, RSTD_STEPS * g + 3)
                nc.vector.scalar_tensor_tensor(newton[:], newton[:], -0.5, var_eps[:], ALU.mult, ALU.mult).then_inc(rstd_step, 1)
                dve.wait_ge(rstd_step, RSTD_STEPS * g + 4)
                nc.vector.scalar_tensor_tensor(rstd[:], newton[:], 1.5, rstd[:], ALU.add, ALU.mult).then_inc(rstd_step, 1)
                dve.wait_ge(rstd_step, RSTD_STEPS * g + 5)
                for n in range(GT):
                    t = GT * g + n
                    dve.wait_ge(h_psum, t + 1)
                    nc.vector.scalar_tensor_tensor(h_ext[:, t], h_acc[:, n, 0:NE], rstd[:, n:n + 1], b_ext[:],
                                                   ALU.mult, ALU.add).then_inc(h_ready, 1)

            normalise(0, 0)
            normalise(0, 1)
            finish(0, 0)
            with dve.Fori(1, NG // 2) as w:
                normalise(w, 0)
                finish(w - 1, 1)
                normalise(w, 1)
                finish(w, 0)
            invert_std(NG - 1, 1)
            finish(NG // 2 - 1, 1)

            dve.wait_ge(h_ready, NT)
            nc.vector.tensor_reduce(s_max[:], h_ext[:, :, D], AX.X, ALU.max).then_inc(s_max_ready, 1)

            def make_mask(u, parity, f):
                i = 2 * u + parity
                slot = F * parity + f
                dve.wait_ge(raw_in[slot // 2], 16 * Q * (u + 1))
                wait(dve, transposed, F * (i - 1) + f + 1)
                nc.vector.tensor_scalar(mask[:, f], raw[:, slot], 0.0, None, ALU.is_gt).then_inc(masked, 1)

            def transpose_mask(u, parity, f):
                i = 2 * u + parity
                dve.wait_ge(masked, F * i + f + 1)
                wait(dve, summed, i - 1)
                nc.vector.transpose(turned[:, parity, :, f], words[:, f]).then_inc(transposed, 1)

            for f in range(F):
                make_mask(0, 0, f)
            dve.wait_ge(part_sum, NG)
            nc.vector.tensor_reduce(h_sum[:], h_part[:, :, 0:D].rearrange("p n d -> p d n"), AX.X, ALU.add).then_inc(h_sum_ready, 1)
            dve.wait_ge(m_ready, 1)
            nc.vector.tensor_scalar(neg_m[:], m_all[:], -1.0, None, ALU.mult).then_inc(neg_m_ready, 1)
            for f in range(F):
                transpose_mask(0, 0, f)
            dve.wait_ge(e_ready, 1)
            dve.wait_ge(bound_step, 4)
            nc.vector.tensor_scalar(es[:], e[:], e_scale[:, 0:1], None, ALU.mult).then_inc(es_ready, 1)
            nc.vector.tensor_scalar(h_ext[:, :, D], e[:], 0.0, h_bound[:, 0:1], ALU.mult, ALU.add).then_inc(es_ready, 1)
            for f in range(F):
                make_mask(0, 1, f)
            dve.wait_ge(h_sum_ready, 1)
            for f in range(F):
                transpose_mask(0, 1, f)
            dve.wait_ge(h_mean_psum, 1)
            nc.vector.tensor_copy(h_mean[:], acc[:, 1, 0, 0:D]).then_inc(h_mean_ready, 1)
            dve.wait_ge(es_ready, 2)

            def leave_rest(t, slot):
                dve.wait_ge(hi_ready, t + 1)
                wait(dve, split_done, t - RESTS + 1)
                nc.vector.scalar_tensor_tensor(rest[:, slot], h_ext[:, t, 0:NV], es[:, bass.ds(t, 1)], parts[:, t, 0, 0:NV],
                                               ALU.mult, ALU.subtract).then_inc(rest_ready, 1)

            def low_part(t, slot):
                dve.wait_ge(rest_ready, t + 1)
                nc.vector.tensor_scalar(parts[:, t, 1, 0:NV], rest[:, slot], LO_SCALE, None, ALU.mult).then_inc(split_done, 1)

            leave_rest(0, 0)
            for n in range(1, RESTS):
                leave_rest(n, n)
                low_part(n - 1, n - 1)
            with dve.Fori(1, NT // RESTS) as w:
                for n in range(RESTS):
                    leave_rest(RESTS * w + n, n)
                    low_part(RESTS * w + n - 1, (n - 1) % RESTS)
            low_part(NT - 1, RESTS - 1)

            def epilogue(u, half):
                i = 2 * u + half
                dve.wait_ge(summed, i + 1)
                nc.vector.tensor_scalar(lo_sum[:], acc[:, half, 1, 0:NV], 1.0 / LO_SCALE, None, ALU.mult).then_inc(epi_step, 1)
                dve.wait_ge(epi_step, EPI_STEPS * i + 1)
                nc.vector.tensor_tensor(total[:], acc[:, half, 0, 0:NV], lo_sum[:], ALU.add).then_inc(acc_read, 1)
                dve.wait_ge(acc_read, i + 1)
                nc.vector.tensor_scalar(den[:], total[:, D:NV], TINY, inv_bound[:, 0:1], ALU.max, ALU.mult).then_inc(epi_step, 1)
                nc.vector.tensor_scalar(lonely[:], total[:, D:NV], 0.0, None, ALU.is_equal).then_inc(epi_step, 1)
                dve.wait_ge(epi_step, EPI_STEPS * i + 3)
                nc.vector.reciprocal(rden[:], den[:]).then_inc(epi_step, 1)
                dve.wait_ge(x_res_in[half], 16 * (u + 1))
                nc.vector.scalar_tensor_tensor(base[:], h_mean[:], lonely[:, 0:1], x_res[:, half], ALU.mult, ALU.add).then_inc(epi_step, 1)
                dve.wait_ge(epi_step, EPI_STEPS * i + 5)
                wait(dve, stored[half], 16 * u)
                nc.vector.scalar_tensor_tensor(y_out[:, half], total[:, 0:D], rden[:, 0:1], base[:], ALU.mult, ALU.add).then_inc(out_ready, 1)

            def pair(u):
                for parity in range(2):
                    for f in range(F):
                        make_mask(u, parity, f)
                    epilogue(u - 1, parity)
                    for f in range(F):
                        transpose_mask(u, parity, f)

            pair(1)
            with dve.Fori(2, PAIRS) as u:
                pair(u)
            for parity in range(2):
                epilogue(PAIRS - 1, parity)


_INS = ["x", "adj", "L0_gnn_W_fc", "L0_gnn_b_fc", "L0_gnn_w_att"]


def kernel(**inputs):
    import numpy as np
    import concourse.bacc as bacc
    from concourse.bass_utils import run_bass_kernel_spmd

    nc = bacc.Bacc("TRN2", target_bir_lowering=False, num_devices=1)
    arrays, args = {}, []
    for name in _INS:
        a = np.ascontiguousarray(inputs[name])
        arrays[name] = a
        args.append(nc.dram_tensor(name, a.shape, mybir.dt.from_np(a.dtype), kind="ExternalInput").ap())
    args.append(nc.dram_tensor("out", (N, D), F32, kind="ExternalOutput").ap())
    build(nc, *args)
    r = run_bass_kernel_spmd(nc, [arrays], core_ids=[0])
    return r.results[0]["out"]
```

```python
from contextlib import ExitStack

import concourse.bass as bass
from concourse import mybir

ALU = mybir.AluOpType
ACT = mybir.ActivationFunctionType
AX = mybir.AxisListType
F32, F16, I32 = mybir.dt.float32, mybir.dt.float16, mybir.dt.int32

P = 128
N = 8192
D = 256
NT = N // P
KH = D // P
LN_EPS = 1e-5
NV = D + 1
NE = D + 2

GT = 4
NG = NT // GT
DC = GT // 2

Q = 4
QP = P // Q
F = P // QP
CW = N // Q
CWORDS = CW // 2
PAIRS = NT // 2
EVEN_FIRST, ODD_FIRST = (0, 2), (3, 1)
HALVES = 2
RAW = 2 * F
UNROLL = 8
POOL_PART = 2
DVE_PARTS = [0, 1, 3]
LAST_PIECE = 12
PIECES = [(0, 2), (2, 4)] + [(t, t + 4) for t in range(4, NT - LAST_PIECE, 4)] + [(NT - LAST_PIECE, NT)]
SHIFT = 8
TOP = 32768.0
TINY = 1e-20
RSTD_STEPS = 5
EPI_STEPS = 5

NEG_INF = -1e9
MAX_SPREAD = 6.0
MAX_DEPTH = 1e8
MIN_G, MAX_G = 1e-12, 1e15
GEN_STEPS = 7


def build(nc, x, adj, w_fc, b_fc, w_att, b_att, scratch, out):
    with ExitStack() as ctx:
        def sb(name, shape, dt=F32):
            return ctx.enter_context(nc.sbuf_tensor(name, shape, dt))

        def sem(name):
            return ctx.enter_context(nc.semaphore(name))

        g_mem = sb("g_mem", [P, SHIFT + NT, NE])
        raw = sb("raw", [P, RAW, CW], I32)
        mask = sb("mask", [P, F, CW], F16)
        turned = sb("turned", [P, 2, CWORDS // QP, F, QP], I32)
        stats = sb("stats", [P, GT, 6])
        mean_var = sb("mean_var", [P, 2, GT, 2])
        neg_mean = sb("neg_mean", [P, 2, GT - DC])
        std = sb("std", [P, NT])
        rstd = sb("rstd", [P, NT])
        var_eps = sb("var_eps", [P, GT])
        newton = sb("newton", [P, GT])
        y_t = sb("y_t", [P, 2, NE])
        w_ext = sb("w_ext", [P, KH, NE])
        wa_b = sb("wa_b", [P, 2 * D])
        b_all = sb("b_all", [P, D])
        g_part = sb("g_part", [P, GT, D])
        ident = sb("ident", [P, P])
        ones_n = sb("ones_n", [P, P])
        eps = sb("eps", [P, 1])
        w_norm_sq = sb("w_norm_sq", [P, 1])
        w_norm = sb("w_norm", [P, 1])
        g_bound = sb("g_bound", [P, 1])
        inv_bound = sb("inv_bound", [P, 1])
        e_scale = sb("e_scale", [P, 1])
        extremes = sb("extremes", [P, 3])
        least = sb("least", [P, 2])
        extremes_all = sb("extremes_all", [P, 3])
        shift_terms = sb("shift_terms", [P, 3])
        row_shift = sb("row_shift", [P, 1])
        checks = sb("checks", [P, 4])
        direct = sb("direct", [P, 1], I32)
        neg_m = sb("neg_m", [P, 1])
        s_dst = sb("s_dst", [P, NT])
        e = sb("e", [P, NT])
        es = sb("es", [P, NT])
        den = sb("den", [P, 1])
        rden = sb("rden", [P, 1])
        lonely = sb("lonely", [P, 1])
        late = sb("late", [P, 2 * GT, D])

        g_ext = g_mem[:, SHIFT:]
        parts = g_mem[:].rearrange("p t c -> p (t c)").bitcast(F16).rearrange("p (t h c) -> p t h c", h=2, c=NE)
        words = mask[:].rearrange("p f c -> p (f c)").bitcast(I32).rearrange("p (f a t) -> p f t a", f=F, a=QP)
        at = turned[:].rearrange("p h t f b -> p (h t f b)").bitcast(F16).rearrange("p (h t m r) -> p h t m r", h=2, m=P, r=2)
        x_in = [g_mem[:, GT * k:GT * (k + 1)].rearrange("p t c -> p (t c)")[:, 0:GT * D].rearrange("p (n d) -> p n d", n=GT)
                for k in range(2)]
        scaled = y_t[:, :, 0:NV]
        y = late[:].rearrange("p (k n) d -> p k n d", k=2)
        x_res, y_out = late[:, 0:2], late[:, 2:4]
        shifted = late[:, 4]
        base = late[:, 5]
        g_sum, g_mean = late[:, 6], late[:, 7]
        w_work = raw[:, F + 2].bitcast(F32).rearrange("p (j k d) -> p j k d", j=4, k=KH)
        w_prod, w_sq = w_work[:, 0:2], w_work[:, 2]

        gen_adj = raw[:, 0:F].rearrange("p f c -> p (f c)")
        gen_edge = gen_adj.bitcast(F32)
        gen_scores = raw[:, F:RAW].rearrange("p f c -> p (f c)").bitcast(F32)
        gen_blocks = gen_scores.rearrange("p (a t) -> p t a", t=NT)
        gen_s_dst = turned[:].rearrange("p h t f b -> p (h t f b)").bitcast(F32)
        gen_turned = y_t[:, :, 0:P]
        row_max, neg_row_max = den, lonely

        acc = ctx.enter_context(nc.psum_tensor("acc", [P, 2, 512], F32))
        turn_acc = ctx.enter_context(nc.psum_tensor("turn_acc", [P, 2, 512], F32))
        g_acc = ctx.enter_context(nc.psum_tensor("g_acc", [P, GT, 512], F32))

        weights_in = sem("weights_in")
        x_in_s = [[sem(f"x_in_{k}_{who}") for who in ("dve", "act")] for k in range(2)]
        raw_in = [sem(f"raw_in_{k}") for k in range(RAW // 2)]
        x_res_in = [sem(f"x_res_in_{k}") for k in range(2)]
        stored = [sem(f"stored_{k}") for k in range(2)]
        ident_ready = sem("ident_ready")
        consts = sem("consts")
        w_ready = sem("w_ready")
        w_sq_ready = sem("w_sq_ready")
        norms_psum = sem("norms_psum")
        norm_max = sem("norm_max")
        norm_root = sem("norm_root")
        bound_step = sem("bound_step")
        stats_done = sem("stats_done")
        var_ready = sem("var_ready")
        std_ready = sem("std_ready")
        rstd_step = sem("rstd_step")
        neg_mean_ready = sem("neg_mean_ready")
        y_dve = sem("y_dve")
        y_act = sem("y_act")
        yt_psum = sem("yt_psum")
        yt_ready = sem("yt_ready")
        g_psum = sem("g_psum")
        g_ready = sem("g_ready")
        part_sum = sem("part_sum")
        g_sum_ready = sem("g_sum_ready")
        g_mean_psum = sem("g_mean_psum")
        g_mean_ready = sem("g_mean_ready")
        extremes_ready = sem("extremes_ready")
        extremes_all_ready = sem("extremes_all_ready")
        neg_m_ready = sem("neg_m_ready")
        s_dst_kept = sem("s_dst_kept")
        e_ready = sem("e_ready")
        es_ready = sem("es_ready")
        hi_ready = sem("hi_ready")
        lo_dve = sem("lo_dve")
        scaled_ready = sem("scaled_ready")
        lo_pool = sem("lo_pool")
        masked = sem("masked")
        transposed = sem("transposed")
        summed = sem("summed")
        epi_step = sem("epi_step")
        out_ready = sem("out_ready")
        shift_step = sem("shift_step")
        check_step = sem("check_step")
        gen_setup = sem("gen_setup")
        gen_scratch = sem("gen_scratch")
        gen_s_dst_in = sem("gen_s_dst_in")
        gen_adj_in = sem("gen_adj_in")
        gen_x_in = sem("gen_x_in")
        gen_step = sem("gen_step")
        gen_exp = sem("gen_exp")
        gen_turn_psum = sem("gen_turn_psum")
        gen_turn_ready = sem("gen_turn_ready")
        gen_product = sem("gen_product")
        gen_rest = sem("gen_rest")
        gen_out = sem("gen_out")
        gen_stored = sem("gen_stored")

        x_groups = x.rearrange("(p g n) d -> g p n d", p=P, n=GT)
        x_tiles = x.rearrange("(i p) d -> i p d", p=P)
        out_tiles = out.rearrange("(i p) d -> i p d", p=P)
        adj_quarters = adj.rearrange("(i f b) (q c) -> i q b f c", f=F, b=QP, q=Q)

        adj_rows = adj.rearrange("(p t) j -> t p j", t=NT)
        x_rows = x.rearrange("(p t) d -> t p d", t=NT)
        out_rows = out.rearrange("(p t) d -> t p d", t=NT)

        def load_adjacency(eng, i, slot, half, quadrants):
            for q in quadrants:
                eng.dma_start(raw[q * QP:(q + 1) * QP, slot:slot + 2],
                              adj_quarters[i, q, :, 2 * half:2 * half + 2]).then_inc(raw_in[slot // 2], 16)

        def wait(eng, s, count):
            if not isinstance(count, int) or count > 0:
                eng.wait_ge(s, count)

        def is_direct(eng):
            eng.wait_ge(check_step, 6)
            return eng.value_load(direct[0:1, 0:1], min_val=0, max_val=1)

        block = ctx.enter_context(nc.Block())

        @block.sync
        def _(sp):
            def load_x(w):
                for k in range(2):
                    wait(sp, y_dve, DC * (2 * w + k - 1))
                    sp.dma_start(x_in[k][:, 0:DC], x_groups[2 * w + k][:, 0:DC]).then_inc(x_in_s[k][0], 16)
                    wait(sp, y_act, (GT - DC) * (2 * w + k - 1))
                    sp.dma_start(x_in[k][:, DC:GT], x_groups[2 * w + k][:, DC:GT]).then_inc(x_in_s[k][1], 16)

            def load_tile(u, parity, halves=range(HALVES)):
                for half in halves:
                    wait(sp, masked, F * (2 * u + parity - 2) + 2 * half + 2)
                    load_adjacency(sp, 2 * u + parity, F * parity + 2 * half, half, EVEN_FIRST)

            load_x(0)
            load_adjacency(sp, 0, 0, 0, EVEN_FIRST)
            load_x(1)
            load_adjacency(sp, 0, 2, 1, EVEN_FIRST)
            load_x(2)
            load_adjacency(sp, 1, 4, 0, EVEN_FIRST)
            load_x(3)
            sp.wait_ge(shift_step, 2)
            sp.wait_ge(norms_psum, 1)
            load_adjacency(sp, 1, 6, 1, EVEN_FIRST)
            load_x(4)
            load_tile(1, 0, halves=(0,))
            load_x(5)
            load_tile(1, 0, halves=(1,))
            with sp.Fori(6, NG // 2) as w:
                load_x(w)

            def store(i, slot):
                sp.wait_ge(out_ready, i + 1)
                sp.dma_start(out_tiles[i], y_out[:, slot]).then_inc(stored[slot], 16)

            def load_residual(i, slot):
                wait(sp, out_ready, i - 1)
                sp.dma_start(x_res[:, slot], x_tiles[i]).then_inc(x_res_in[slot], 16)

            load_tile(1, 1)

            def direct_rows():
                for parity in range(2):
                    load_residual(parity, parity)
                with sp.Fori(2, PAIRS) as u:
                    for parity in range(2):
                        load_tile(u, parity)
                        store(2 * u + parity - 4, parity)
                        load_residual(2 * u + parity - 2, parity)
                for i in range(NT - 4, NT):
                    store(i, i % 2)
                    if i + 2 < NT:
                        load_residual(i + 2, i % 2)
                for slot in range(2):
                    sp.wait_ge(stored[slot], 16 * (NT // 2))

            def general_rows():
                sp.wait_ge(s_dst_kept, 1)
                sp.dma_start(scratch.rearrange("(p t) -> p t", t=NT), s_dst[:]).then_inc(gen_scratch, 16)
                sp.wait_ge(gen_scratch, 16)
                sp.wait_ge(transposed, 2 * F)
                sp.dma_start(gen_s_dst, scratch.partition_broadcast(P)).then_inc(gen_s_dst_in, 16)
                for slot in range(RAW // 2):
                    sp.wait_ge(raw_in[slot], 16 * Q * 2)

                def row_tile(w):
                    wait(sp, gen_step, GEN_STEPS * (w - 1) + 4)
                    sp.dma_start(gen_adj, adj_rows[w]).then_inc(gen_adj_in, 16)
                    wait(sp, gen_out, w)
                    sp.dma_start(x_res[:, 0], x_rows[w]).then_inc(gen_x_in, 16)
                    sp.wait_ge(gen_out, w + 1)
                    sp.dma_start(out_rows[w], y_out[:, 0]).then_inc(gen_stored, 16)

                row_tile(0)
                with sp.Fori(1, NT) as w:
                    row_tile(w)
                sp.wait_ge(gen_stored, 16 * NT)

            with sp.If(is_direct(sp) > 0):
                direct_rows()
            with sp.Else():
                general_rows()

        @block.gpsimd
        def _(pool):
            nc.gpsimd.memset(ident[:], 0.0).then_inc(ident_ready, 1)
            pool.wait_ge(ident_ready, 1)
            nc.gpsimd.affine_select(out=ident[:], in_=ident[:], compare_op=ALU.not_equal, fill=1.0, base=0,
                                    pattern=[[-1, P]], channel_multiplier=1).then_inc(ident_ready, 1)
            pool.wait_ge(g_ready, GT)
            nc.gpsimd.tensor_copy(g_part[:], g_ext[:, 0:GT, 0:D]).then_inc(part_sum, 1)

            def add_group(g):
                pool.wait_ge(g_ready, GT * (g + 1))
                pool.wait_ge(part_sum, g)
                nc.gpsimd.tensor_tensor(g_part[:], g_part[:], g_ext[:, bass.ds(g * GT, GT), 0:D], ALU.add).then_inc(part_sum, 1)

            with pool.Fori(1, NG - 1) as g:
                add_group(g)
            pool.wait_ge(extremes_ready, 3)
            nc.gpsimd.partition_all_reduce(extremes_all[:], extremes[:], P, bass.bass_isa.ReduceOp.max).then_inc(extremes_all_ready, 1)
            add_group(NG - 1)

            def low_parts(w):
                for half in range(2):
                    g = 2 * w + half
                    t = 4 * g + POOL_PART
                    pool.wait_ge(hi_ready, t + 1)
                    wait(pool, lo_pool, g - 1)
                    nc.gpsimd.tensor_tensor(scaled[:, half], g_ext[:, t, 0:NV], es[:, bass.ds(t, 1)].to_broadcast([P, NV]),
                                            ALU.mult).then_inc(scaled_ready, 1)
                    pool.wait_ge(scaled_ready, g + 1)
                    nc.gpsimd.tensor_tensor(parts[:, t, 1, 0:NV], scaled[:, half], parts[:, t, 0, 0:NV],
                                            ALU.subtract).then_inc(lo_pool, 1)

            low_parts(0)
            with pool.If(is_direct(pool) > 0):
                with pool.Fori(1, NT // UNROLL) as w:
                    low_parts(w)

        @block.tensor
        def _(pe):
            pe.wait_ge(ident_ready, 2)

            def turn(w, m):
                t = 2 * GT * w + m
                g, n = 2 * w + m // GT, m % GT
                if n < DC:
                    pe.wait_ge(y_dve, DC * g + n + 1)
                else:
                    pe.wait_ge(y_act, (GT - DC) * g + n - DC + 1)
                wait(pe, yt_ready, t - 1)
                for k in range(KH):
                    mm = nc.tensor.transpose(turn_acc[:, m % 2, k * P:(k + 1) * P],
                                             y[:, m // GT % 2, m % GT, k * P:(k + 1) * P], ident[:])
                mm.then_inc(yt_psum, 1)

            def times_w(w, m):
                t = 2 * GT * w + m
                pe.wait_ge(yt_ready, t + 1)
                wait(pe, g_ready, t - GT + 1)
                for k in range(KH):
                    mm = nc.tensor.matmul(g_acc[:, m % GT, 0:NE], y_t[:, m % 2, k * P:(k + 1) * P], w_ext[:, k],
                                          start=(k == 0), stop=(k == KH - 1))
                mm.then_inc(g_psum, 1)

            def two_groups(w, last=False):
                for m in range(2 * GT):
                    if not (last and m == 2 * GT - 1):
                        turn(w, m + 1)
                    times_w(w, m)

            turn(0, 0)
            pe.wait_ge(w_ready, 1)
            two_groups(0)
            pe.wait_ge(w_sq_ready, 1)
            pe.wait_ge(consts, 2)
            for k in range(KH):
                mm = nc.tensor.matmul(acc[:, 0, 0:D], ones_n[:], w_sq[:, k], start=(k == 0), stop=(k == KH - 1))
            mm.then_inc(norms_psum, 1)
            with pe.Fori(1, NG // 2 - 1) as w:
                two_groups(w)
            two_groups(NG // 2 - 1, last=True)

            def product(parity, t, part):
                return nc.tensor.matmul(acc[:, parity, 0:NV], at[:, parity, t // 2, :, t % 2], parts[:, t, part, 0:NV],
                                        start=(t == 0 and part == 0), stop=(t == NT - 1 and part == 1))

            def direct_products():
                pe.wait_ge(transposed, 2 * F)
                for first, end in PIECES:
                    from_pool = sum(t % 4 == POOL_PART for t in range(end))
                    pe.wait_ge(lo_dve, end - from_pool)
                    wait(pe, lo_pool, from_pool)
                    for parity in range(2):
                        for t in range(first, end):
                            for part in range(2):
                                mm = product(parity, t, part)
                        if end == NT:
                            mm.then_inc(summed, 1)
                    if end == NT - LAST_PIECE:
                        pe.wait_ge(g_sum_ready, 1)
                        nc.tensor.matmul(g_acc[:, 0, 0:D], ones_n[:], g_sum, start=True, stop=True).then_inc(g_mean_psum, 1)

                with pe.Fori(1, PAIRS) as u:
                    for parity in range(2):
                        i = 2 * u + parity
                        pe.wait_ge(transposed, F * (i + 1))
                        pe.wait_ge(out_ready, i - 1)
                        for t in range(NT):
                            for part in range(2):
                                mm = product(parity, t, part)
                        mm.then_inc(summed, 1)

            def general_products():
                pe.wait_ge(g_ready, NT)
                pe.wait_ge(gen_setup, 2)

                def row_tile(w):
                    pe.wait_ge(gen_exp, w + 1)
                    wait(pe, gen_out, w)
                    for t in range(NT + 1):
                        if t < NT:
                            wait(pe, gen_turn_ready, NT * w + t - 1)
                            nc.tensor.transpose(turn_acc[:, t % 2, 0:P], gen_blocks[:, t], ident[:]).then_inc(gen_turn_psum, 1)
                        if t > 0:
                            pe.wait_ge(gen_turn_ready, NT * w + t)
                            nc.tensor.matmul(acc[:, 0, 0:NV], gen_turned[:, (t - 1) % 2], g_ext[:, t - 1, 0:NV],
                                             start=(t == 1), stop=(t == NT)).then_inc(gen_product, 1)

                row_tile(0)
                with pe.Fori(1, NT) as w:
                    row_tile(w)

            with pe.If(is_direct(pe) > 0):
                direct_products()
            with pe.Else():
                general_products()

        @block.scalar
        def _(act):
            act.dma_start(w_ext[:, :, 0:D], w_fc.rearrange("(k p) d -> p k d", p=P)).then_inc(weights_in, 16)
            act.dma_start(wa_b[:], w_att.partition_broadcast(P)).then_inc(weights_in, 16)
            act.dma_start(b_all[:], b_fc.partition_broadcast(P)).then_inc(weights_in, 16)
            act.dma_start(shift_terms[:, 0:1], b_att.partition_broadcast(P)).then_inc(weights_in, 16)
            load_adjacency(act, 0, 0, 0, ODD_FIRST)
            act.wait_ge(consts, 2)

            def deviation(w, k):
                g = 2 * w + k
                act.wait_ge(var_ready, GT * (g + 1))
                nc.scalar.activation(std[:, bass.ds(GT * g, GT)], mean_var[:, k, :, 1], ACT.Sqrt, bias=eps[:, 0:1]).then_inc(std_ready, 1)

            def centre(w, k, n):
                g = 2 * w + k
                act.wait_ge(neg_mean_ready, g + 1)
                wait(act, yt_psum, GT * (g - 1))
                nc.scalar.activation(y[:, k, n], x_in[k][:, n], ACT.Relu, bias=neg_mean[:, k, n - DC:n - DC + 1]).then_inc(y_act, 1)

            def turned_y(t, slot):
                act.wait_ge(yt_psum, t + 1)
                wait(act, g_psum, t - 1)
                nc.scalar.activation(y_t[:, slot, 0:D], turn_acc[:, slot, 0:D], ACT.Copy).then_inc(yt_ready, 1)

            def scaled_g(g, n):
                act.wait_ge(g_psum, GT * g + n + 1)
                act.wait_ge(rstd_step, RSTD_STEPS * (g + 1))
                nc.scalar.activation(g_ext[:, GT * g + n], g_acc[:, n, 0:NE], ACT.Copy, scale=rstd[:, bass.ds(GT * g + n, 1)]).then_inc(g_ready, 1)

            def group(w, k, last=False):
                g = 2 * w + k
                for n in range(GT):
                    turned_y(GT * g + n, n % 2)
                    if not isinstance(g, int) or g > 0:
                        scaled_g(g - 1, n)
                    if n == 0 and not last:
                        deviation(w + k, 1 - k)
                    if 1 <= n <= GT - DC and not last:
                        centre(w + k, 1 - k, DC + n - 1)

            deviation(0, 0)
            for n in range(DC, GT):
                centre(0, 0, n)
            group(0, 0)
            load_adjacency(act, 0, 2, 1, ODD_FIRST)
            group(0, 1)
            load_adjacency(act, 1, 4, 0, ODD_FIRST)

            def load_ahead(parity, half):
                act.wait_ge(masked, F * parity + 2 * half + 2)
                load_adjacency(act, 2 + parity, F * parity + 2 * half, half, ODD_FIRST)

            with act.Fori(1, 3) as w:
                for k in range(2):
                    group(w, k)
            act.wait_ge(shift_step, 2)
            act.wait_ge(norms_psum, 1)
            load_adjacency(act, 1, 6, 1, ODD_FIRST)
            for k in range(2):
                group(3, k)
            act.wait_ge(norm_max, 1)
            nc.scalar.activation(w_norm[:], w_norm_sq[:], ACT.Sqrt, scale=float(D * N)).then_inc(norm_root, 1)
            load_ahead(0, 0)
            with act.Fori(4, 6) as w:
                for k in range(2):
                    group(w, k)
            load_ahead(0, 1)
            with act.Fori(6, NG // 2 - 1) as w:
                for k in range(2):
                    group(w, k)
            group(NG // 2 - 1, 0)
            group(NG // 2 - 1, 1, last=True)
            for n in range(GT):
                scaled_g(NG - 1, n)
            act.preload_act_table(ACT.Exp)

            act.wait_ge(neg_m_ready, 1)
            nc.scalar.activation(e[:], g_ext[:, :, D], ACT.Exp, bias=neg_m[:, 0:1]).then_inc(e_ready, 1)

            def high_part(w, n):
                t = UNROLL * w + n
                before = UNROLL // 4 * w + (n - SHIFT) // 4
                if n % 4 == POOL_PART:
                    wait(act, lo_pool, before + 1)
                else:
                    wait(act, lo_dve, 3 * before + DVE_PARTS.index(n % 4) + 1)
                nc.scalar.activation(parts[:, t, 0, 0:NV], g_ext[:, t, 0:NV], ACT.Copy, scale=es[:, bass.ds(t, 1)]).then_inc(hi_ready, 1)

            act.wait_ge(es_ready, 2)
            for n in range(SHIFT):
                high_part(0, n)
            for half in range(HALVES):
                load_ahead(1, half)

            def direct_parts():
                with act.Fori(1, NT // UNROLL - 1) as w:
                    for n in range(UNROLL):
                        high_part(w, n)
                act.wait_ge(part_sum, NG)
                for n in range(UNROLL):
                    high_part(NT // UNROLL - 1, n)

                with act.Fori(2, PAIRS) as u:
                    for parity in range(2):
                        for half in range(HALVES):
                            act.wait_ge(masked, F * (2 * u + parity - 2) + 2 * half + 2)
                            load_adjacency(act, 2 * u + parity, F * parity + 2 * half, half, ODD_FIRST)

            def general_exponentials():
                def row_tile(w):
                    act.wait_ge(gen_step, GEN_STEPS * w + 6)
                    nc.scalar.activation(gen_scores, gen_scores, ACT.Exp, bias=neg_row_max[:, 0:1]).then_inc(gen_exp, 1)
                    for t in range(NT):
                        act.wait_ge(gen_turn_psum, NT * w + t + 1)
                        wait(act, gen_product, NT * w + t - 1)
                        nc.scalar.activation(gen_turned[:, t % 2], turn_acc[:, t % 2, 0:P], ACT.Copy).then_inc(gen_turn_ready, 1)

                row_tile(0)
                with act.Fori(1, NT) as w:
                    row_tile(w)

            with act.If(is_direct(act) > 0):
                direct_parts()
            with act.Else():
                general_exponentials()

        @block.vector
        def _(dve):
            nc.vector.memset(ones_n[:], 1.0 / N).then_inc(consts, 1)
            nc.vector.memset(eps[:], LN_EPS).then_inc(consts, 1)

            def statistics(g, k, n):
                nc.vector.bn_stats(stats[:, n], x_in[k][:, n]).then_inc(stats_done, 1)

            def aggregate(k, n):
                nc.vector.bn_aggr(mean_var[:, k, n], stats[:, n]).then_inc(var_ready, 1)

            def centre(k, n):
                nc.vector.tensor_scalar(y[:, k, n], x_in[k][:, n], mean_var[:, k, n, 0:1], 0.0,
                                        ALU.subtract, ALU.max).then_inc(y_dve, 1)

            def newton_step(g, k, step):
                group_rstd = rstd[:, GT * g:GT * (g + 1)]
                if step == 0:
                    dve.wait_ge(std_ready, g + 1)
                    nc.vector.reciprocal(group_rstd, std[:, GT * g:GT * (g + 1)]).then_inc(rstd_step, 1)
                if step == 1:
                    dve.wait_ge(rstd_step, RSTD_STEPS * g + 1)
                    nc.vector.tensor_tensor(newton[:], group_rstd, group_rstd, ALU.mult).then_inc(rstd_step, 1)
                    nc.vector.tensor_scalar(var_eps[:], mean_var[:, k, :, 1], LN_EPS, None, ALU.add).then_inc(rstd_step, 1)
                if step == 2:
                    dve.wait_ge(rstd_step, RSTD_STEPS * g + 3)
                    nc.vector.scalar_tensor_tensor(newton[:], newton[:], -0.5, var_eps[:], ALU.mult, ALU.mult).then_inc(rstd_step, 1)
                if step == 3:
                    dve.wait_ge(rstd_step, RSTD_STEPS * g + 4)
                    nc.vector.scalar_tensor_tensor(group_rstd, newton[:], 1.5, group_rstd, ALU.add, ALU.mult).then_inc(rstd_step, 1)

            def group(w, k, meanwhile=None):
                g = 2 * w + k
                before = not isinstance(g, int) or g > 0
                for n in range(GT + 1):
                    if n == 0:
                        dve.wait_ge(x_in_s[k][0], 16 * (w + 1))
                    if n == DC:
                        dve.wait_ge(x_in_s[k][1], 16 * (w + 1))
                    if n < GT:
                        statistics(g, k, n)
                        if before:
                            newton_step(g - 1, 1 - k, n)
                    if n > 0:
                        dve.wait_ge(stats_done, GT * g + n)
                        aggregate(k, n - 1)
                dve.wait_ge(var_ready, GT * (g + 1))
                wait(dve, y_act, (GT - DC) * (g - 1))
                nc.vector.tensor_scalar(neg_mean[:, k], mean_var[:, k, DC:GT, 0], -1.0, None, ALU.mult).then_inc(neg_mean_ready, 1)
                if meanwhile is not None:
                    first_masks(meanwhile)
                wait(dve, yt_psum, GT * (g - 1))
                for n in range(DC):
                    centre(k, n)

            def weights():
                dve.wait_ge(weights_in, 64)
                for j, half in ((0, 1), (1, 0)):
                    for k in range(KH):
                        last = nc.vector.tensor_tensor_reduce(out=w_prod[:, j, k], in0=w_ext[:, k, 0:D],
                                                              in1=wa_b[:, half * D:(half + 1) * D],
                                                              scale=1.0, scalar=0.0, op0=ALU.mult, op1=ALU.add,
                                                              accum_out=w_ext[:, k, D + j:D + j + 1])
                last.then_inc(w_ready, 1)

            def squares():
                nc.vector.tensor_tensor(w_sq, w_ext[:, :, 0:D], w_ext[:, :, 0:D], ALU.mult).then_inc(w_sq_ready, 1)

            def shift():
                dve.wait_ge(w_ready, 1)
                for j in range(2):
                    nc.vector.tensor_tensor_reduce(out=w_prod[:, j, 0], in0=b_all[:], in1=wa_b[:, j * D:(j + 1) * D],
                                                   scale=1.0, scalar=0.0, op0=ALU.mult, op1=ALU.add,
                                                   accum_out=shift_terms[:, 1 + j:2 + j]).then_inc(shift_step, 1)
                dve.wait_ge(shift_step, 2)
                nc.vector.tensor_reduce(row_shift[:], shift_terms[:], AX.X, ALU.add).then_inc(shift_step, 1)

            def largest_norm():
                dve.wait_ge(norms_psum, 1)
                nc.vector.tensor_reduce(w_norm_sq[:], acc[:, 0, 0:D], AX.X, ALU.max).then_inc(norm_max, 1)

            def bound():
                dve.wait_ge(norm_root, 1)
                nc.vector.tensor_scalar(g_bound[:], w_norm[:], TINY, None, ALU.max).then_inc(bound_step, 1)
                dve.wait_ge(bound_step, 1)
                nc.vector.reciprocal(inv_bound[:], g_bound[:]).then_inc(bound_step, 1)
                dve.wait_ge(bound_step, 2)
                nc.vector.tensor_scalar(e_scale[:], inv_bound[:], TOP, None, ALU.mult).then_inc(bound_step, 1)

            def make_mask(i, f, slot, use):
                dve.wait_ge(raw_in[slot // 2], 16 * Q * use)
                wait(dve, transposed, F * (i - 1) + f + 1)
                nc.vector.tensor_scalar(mask[:, f], raw[:, slot], 0.0, None, ALU.is_gt).then_inc(masked, 1)

            def transpose_mask(i, parity, f):
                dve.wait_ge(masked, F * i + f + 1)
                wait(dve, summed, i - 1)
                nc.vector.transpose(turned[:, parity, :, f], words[:, f]).then_inc(transposed, 1)

            def first_masks(j):
                i, f = j // (2 * F), j % F
                if j // F % 2 == 0:
                    make_mask(i, f, F * i + f, 1)
                else:
                    transpose_mask(i, i, f)

            group(0, 0)
            weights()
            group(0, 1)
            squares()
            shift()
            for j in range(2, NG):
                group(j // 2, j % 2, meanwhile=j - 2)
                if j == 4:
                    largest_norm()
                if j == 10:
                    bound()
            for step in range(GT):
                newton_step(NG - 1, 1, step)
            for j in range(NG - 2, 4 * F):
                first_masks(j)

            dve.wait_ge(g_ready, NT)
            nc.vector.tensor_reduce(extremes[:, 0:1], g_ext[:, :, D], AX.X, ALU.max).then_inc(extremes_ready, 1)
            nc.vector.tensor_reduce(least[:], g_ext[:, :, D:NE].rearrange("p t c -> p c t"), AX.X, ALU.min).then_inc(extremes_ready, 1)
            dve.wait_ge(extremes_ready, 2)
            nc.vector.tensor_scalar(extremes[:, 1:3], least[:], -1.0, None, ALU.mult).then_inc(extremes_ready, 1)
            nc.vector.tensor_copy(s_dst[:], g_ext[:, :, D]).then_inc(s_dst_kept, 1)
            dve.wait_ge(extremes_all_ready, 1)
            nc.vector.tensor_scalar(neg_m[:], extremes_all[:, 0:1], -1.0, None, ALU.mult).then_inc(neg_m_ready, 1)

            spread, depth = checks[:, 0:1], checks[:, 1:2]
            nc.vector.tensor_scalar(spread, extremes_all[:, 0:1], extremes_all[:, 1:2], MAX_SPREAD, ALU.add, ALU.is_le).then_inc(check_step, 1)
            dve.wait_ge(bound_step, 3)
            dve.wait_ge(e_ready, 1)
            nc.vector.tensor_scalar(es[:], e[:], e_scale[:, 0:1], None, ALU.mult).then_inc(es_ready, 1)
            nc.vector.tensor_scalar(g_ext[:, :, D], e[:], 0.0, g_bound[:, 0:1], ALU.mult, ALU.add).then_inc(es_ready, 1)
            dve.wait_ge(shift_step, 3)
            nc.vector.scalar_tensor_tensor(depth, extremes_all[:, 1:2], extremes_all[:, 2:3], row_shift[:],
                                           ALU.add, ALU.subtract).then_inc(check_step, 1)
            dve.wait_ge(check_step, 2)
            nc.vector.tensor_scalar(depth, depth, MAX_DEPTH, None, ALU.is_le).then_inc(check_step, 1)
            nc.vector.tensor_scalar(checks[:, 2:3], g_bound[:], MIN_G, None, ALU.is_ge).then_inc(check_step, 1)
            nc.vector.tensor_scalar(checks[:, 3:4], g_bound[:], MAX_G, None, ALU.is_le).then_inc(check_step, 1)
            dve.wait_ge(check_step, 5)
            nc.vector.tensor_reduce(direct[:], checks[:], AX.X, ALU.min).then_inc(check_step, 1)

            def low_part(t):
                dve.wait_ge(hi_ready, t + 1)
                nc.vector.scalar_tensor_tensor(parts[:, t, 1, 0:NV], g_ext[:, t, 0:NV], es[:, bass.ds(t, 1)], parts[:, t, 0, 0:NV],
                                               ALU.mult, ALU.subtract).then_inc(lo_dve, 1)

            def epilogue(u, parity):
                i = 2 * u + parity
                dve.wait_ge(x_res_in[parity], 16 * (u + 1))
                nc.vector.tensor_tensor(shifted, x_res[:, parity], b_all[:], ALU.add).then_inc(epi_step, 1)
                dve.wait_ge(summed, i + 1)
                nc.vector.tensor_scalar(lonely[:], acc[:, parity, D:NV], 0.0, None, ALU.is_equal).then_inc(epi_step, 1)
                nc.vector.tensor_scalar(den[:], acc[:, parity, D:NV], TINY, inv_bound[:, 0:1], ALU.max, ALU.mult).then_inc(epi_step, 1)
                dve.wait_ge(epi_step, EPI_STEPS * i + 3)
                nc.vector.reciprocal(rden[:], den[:]).then_inc(epi_step, 1)
                nc.vector.scalar_tensor_tensor(base, g_mean, lonely[:, 0:1], shifted, ALU.mult, ALU.add).then_inc(epi_step, 1)
                dve.wait_ge(epi_step, EPI_STEPS * i + 5)
                wait(dve, stored[parity], 16 * u)
                nc.vector.scalar_tensor_tensor(y_out[:, parity], acc[:, parity, 0:D], rden[:, 0:1], base,
                                               ALU.mult, ALU.add).then_inc(out_ready, 1)

            def pair(u):
                for parity in range(2):
                    i = 2 * u + parity
                    for f in range(F):
                        make_mask(i, f, F * parity + f, u + 1)
                    epilogue(u - 1, parity)
                    for f in range(F):
                        transpose_mask(i, parity, f)

            def low_parts(w):
                for n in range(UNROLL):
                    if n % 4 != POOL_PART:
                        low_part(UNROLL * w + n)

            dve.wait_ge(es_ready, 2)
            low_parts(0)

            def direct_rows():
                for f in range(F):
                    with dve.Fori(max(1, f * NT // UNROLL // F), (f + 1) * NT // UNROLL // F) as w:
                        low_parts(w)
                    if f == 0:
                        dve.wait_ge(part_sum, NG)
                        nc.vector.tensor_reduce(g_sum, g_part[:].rearrange("p n d -> p d n"), AX.X, ALU.add).then_inc(g_sum_ready, 1)
                    make_mask(2, f, f, 2)
                dve.wait_ge(g_mean_psum, 1)
                nc.vector.tensor_copy(g_mean, g_acc[:, 0, 0:D]).then_inc(g_mean_ready, 1)

                for f in range(F):
                    transpose_mask(2, 0, f)
                epilogue(0, 0)
                for f in range(F):
                    make_mask(3, f, F + f, 2)
                epilogue(0, 1)
                for f in range(F):
                    transpose_mask(3, 1, f)
                with dve.Fori(2, PAIRS) as u:
                    pair(u)
                for parity in range(2):
                    epilogue(PAIRS - 1, parity)

            def general_rows():
                nc.vector.tensor_scalar(e[:], g_ext[:, :, D + 1], row_shift[:, 0:1], None, ALU.add).then_inc(gen_setup, 1)
                dve.wait_ge(lo_dve, SHIFT // 4 * 3)
                dve.wait_ge(lo_pool, SHIFT // 4)
                nc.vector.memset(g_ext[:, :, D], 1.0).then_inc(gen_setup, 1)
                dve.wait_ge(gen_setup, 2)
                dve.wait_ge(gen_s_dst_in, 16)

                def row_tile(w):
                    dve.wait_ge(gen_adj_in, 16 * (w + 1))
                    nc.vector.tensor_scalar(gen_edge, gen_adj, 0.0, None, ALU.is_gt).then_inc(gen_step, 1)
                    dve.wait_ge(gen_step, GEN_STEPS * w + 1)
                    wait(dve, gen_product, NT * w)
                    nc.vector.scalar_tensor_tensor(gen_scores, gen_s_dst, e[:, bass.ds(w, 1)], gen_edge,
                                                   ALU.add, ALU.mult).then_inc(gen_step, 1)
                    dve.wait_ge(gen_step, GEN_STEPS * w + 2)
                    nc.vector.tensor_scalar(gen_edge, gen_edge, 1.0, -NEG_INF, ALU.subtract, ALU.mult).then_inc(gen_step, 1)
                    dve.wait_ge(gen_step, GEN_STEPS * w + 3)
                    nc.vector.tensor_tensor(gen_scores, gen_scores, gen_edge, ALU.add).then_inc(gen_step, 1)
                    dve.wait_ge(gen_step, GEN_STEPS * w + 4)
                    nc.vector.tensor_reduce(row_max[:], gen_scores, AX.X, ALU.max).then_inc(gen_step, 1)
                    dve.wait_ge(gen_step, GEN_STEPS * w + 5)
                    nc.vector.tensor_scalar(neg_row_max[:], row_max[:], -1.0, None, ALU.mult).then_inc(gen_step, 1)
                    dve.wait_ge(gen_x_in, 16 * (w + 1))
                    nc.vector.tensor_tensor(shifted, x_res[:, 0], b_all[:], ALU.add).then_inc(gen_step, 1)
                    dve.wait_ge(gen_product, NT * (w + 1))
                    nc.vector.reciprocal(rden[:], acc[:, 0, D:NV]).then_inc(gen_rest, 1)
                    dve.wait_ge(gen_rest, w + 1)
                    dve.wait_ge(gen_step, GEN_STEPS * (w + 1))
                    wait(dve, gen_stored, 16 * w)
                    nc.vector.scalar_tensor_tensor(y_out[:, 0], acc[:, 0, 0:D], rden[:, 0:1], shifted,
                                                   ALU.mult, ALU.add).then_inc(gen_out, 1)

                row_tile(0)
                with dve.Fori(1, NT) as w:
                    row_tile(w)

            with dve.If(is_direct(dve) > 0):
                direct_rows()
            with dve.Else():
                general_rows()


_INS = ["x", "adj", "L0_gnn_W_fc", "L0_gnn_b_fc", "L0_gnn_w_att", "L0_gnn_b_att"]


def kernel(**inputs):
    import numpy as np
    import concourse.bacc as bacc
    from concourse.bass_utils import run_bass_kernel_spmd

    nc = bacc.Bacc("TRN2", target_bir_lowering=False, num_devices=1)
    arrays, args = {}, []
    for name in _INS:
        a = np.ascontiguousarray(inputs[name])
        if a.ndim == 0:
            a = a.reshape(1)
        arrays[name] = a
        args.append(nc.dram_tensor(name, a.shape, mybir.dt.from_np(a.dtype), kind="ExternalInput").ap())
    args.append(nc.dram_tensor("scratch", (N,), F32, kind="Internal").ap())
    args.append(nc.dram_tensor("out", (N, D), F32, kind="ExternalOutput").ap())
    build(nc, *args)
    r = run_bass_kernel_spmd(nc, [arrays], core_ids=[0])
    return r.results[0]["out"]
```
